# Optimizing a Trainium2 kernel written in Bass

```python
import numpy as np
import jax
import jax.numpy as jnp

def _softmax(x, axis=-1):
    return jax.nn.softmax(x, axis=axis)

def _gelu(x):
    return jax.nn.gelu(x, approximate=True)

def _silu(x):
    return jax.nn.silu(x)

def _sigmoid(x):
    return jax.nn.sigmoid(x)

def _layernorm(x, axis=-1, eps=1e-05):
    m = jnp.mean(x, axis=axis, keepdims=True)
    v = jnp.var(x, axis=axis, keepdims=True)
    return (x - m) / jnp.sqrt(v + eps)

def _scatter_add(tgt, idx, src, axis=0):
    return tgt.at[idx].add(src)

def _segment_sum(src, seg, n):
    return jax.ops.segment_sum(src, seg, n)
kernel_name = 'mk_xattn_ffn_d1_seqx_r4_925c16'

def setup_inputs(seed: int=0):
    np.random.seed(seed)
    _w = jnp.asarray

    def _rec_inputs():
        import jax
        import jax.numpy as jnp
        _rk = jax.random.key(seed)
        x = -0.0003929 + 0.9999 * jax.random.normal(jax.random.fold_in(_rk, 1), (32, 128, 1024), jnp.float32)
        _lenS = 128 - jax.random.randint(jax.random.fold_in(_rk, 7), (32,), 0, max(1, 128 // 4) + 1, jnp.int32)
        _lenS2 = 128 - jax.random.randint(jax.random.fold_in(_rk, 8), (32,), 0, max(1, 128 // 4) + 1, jnp.int32)
        _ctx_1024P = jax.random.normal(jax.random.fold_in(_rk, 11), (32, 16, 256), jnp.float32)
        _ctx_1024c = jax.random.dirichlet(jax.random.fold_in(_rk, 511), 0.3 * jnp.ones((16,), jnp.float32), (32, 128))
        _ctx_1024t = jnp.einsum('bsk,bkd->bsd', _ctx_1024c, _ctx_1024P)
        _ctx_1024t = _ctx_1024t * jax.lax.rsqrt(jnp.mean(jnp.square(_ctx_1024t)) + 1e-12) * 0.953939
        ctx_1024 = -1.39393e-06 + 0.999914 * (_ctx_1024t + 0.3 * jax.random.normal(jax.random.fold_in(_rk, 611), (32, 128, 256), jnp.float32))
        return (x, ctx_1024)
    x, ctx_1024 = _rec_inputs()

    def _L0_xattn_setup():
        import jax, jax.numpy as jnp
        import numpy as np
        import math
        DIM_V = 128
        key = jax.random.key(seed)
        k1, k2, k3, k4, k5, k6 = jax.random.split(key, 6)
        B, C, N, M = (8, DIM_V, 1024, 256)
        pcd_up = jax.random.normal(k1, (B, C, N), dtype=jnp.float32)
        pcd_down = jax.random.normal(k2, (B, C, M), dtype=jnp.float32)
        s = 1.0 / math.sqrt(C)
        Wq = jax.random.normal(k3, (C, C), dtype=jnp.float32) * s
        Wk = jax.random.normal(k4, (C, C), dtype=jnp.float32) * s
        Wv = jax.random.normal(k5, (C, C), dtype=jnp.float32) * s
        Wskip = jax.random.normal(k6, (C, C), dtype=jnp.float32) * s
        return {'pcd_up': pcd_up, 'pcd_down': pcd_down, 'Wq': Wq, 'Wk': Wk, 'Wv': Wv, 'Wskip': Wskip}
    _L0_xattn_all = _L0_xattn_setup()
    _L0_xattn_in = {k: v for k, v in _L0_xattn_all.items() if k in ('Wq', 'Wk', 'Wv', 'Wskip')}
    del _L0_xattn_all

    def _L0_ffn_setup():
        import jax, jax.numpy as jnp
        import numpy as np
        B, S, IN, OUT = (4, 512, 1024, 1024)

        def _dequant_weight(qweight, scales, zeros):
            low = qweight & 15
            high = qweight >> 4 & 15
            w_int = jnp.stack([low, high], axis=1).reshape(-1, qweight.shape[1])
            zp = jnp.round(zeros / scales)
            return (w_int.astype(jnp.float32) - zp.T) * scales.T
        key = jax.random.key(seed)
        k_x, k_q, k_s, k_z, k_b = jax.random.split(key, 5)
        x = jax.random.normal(k_x, (B, S, IN), dtype=jnp.float32)
        qweight = jax.random.randint(k_q, (IN // 2, OUT), 0, 64, dtype=jnp.int32)
        scales = jax.random.uniform(k_s, (OUT, 1), minval=0.01, maxval=0.05, dtype=jnp.float32)
        zeros = jax.random.normal(k_z, (OUT, 1), dtype=jnp.float32) * 0.1
        bias = jax.random.normal(k_b, (OUT,), dtype=jnp.float32) * 0.02
        return {'x': x, 'qweight': qweight, 'scales': scales, 'zeros': zeros, 'bias': bias}
    _L0_ffn_all = _L0_ffn_setup()
    _L0_ffn_in = {k: v for k, v in _L0_ffn_all.items() if k in ('qweight', 'scales', 'zeros', 'bias')}
    del _L0_ffn_all
    return {'x': x, 'ctx_1024': ctx_1024, 'L0_xattn_Wq': _L0_xattn_in['Wq'], 'L0_xattn_Wk': _L0_xattn_in['Wk'], 'L0_xattn_Wv': _L0_xattn_in['Wv'], 'L0_xattn_Wskip': _L0_xattn_in['Wskip'], 'L0_ffn_qweight': _L0_ffn_in['qweight'], 'L0_ffn_scales': _L0_ffn_in['scales'], 'L0_ffn_zeros': _L0_ffn_in['zeros'], 'L0_ffn_bias': _L0_ffn_in['bias']}

def reference(x, ctx_1024, L0_xattn_Wq, L0_xattn_Wk, L0_xattn_Wv, L0_xattn_Wskip, L0_ffn_qweight, L0_ffn_scales, L0_ffn_zeros, L0_ffn_bias):
    import jax
    import jax.numpy as jnp

    def _L0_xattn_ref(pcd_up, pcd_down, Wq, Wk, Wv, Wskip):
        import jax, jax.numpy as jnp
        import numpy as np
        import math
        DIM_V = 128
        q = jnp.einsum('oc,bcn->bon', Wq, pcd_up)
        k = jnp.einsum('oc,bcm->bom', Wk, pcd_down)
        v = jnp.einsum('oc,bcm->bom', Wv, pcd_down)
        C = q.shape[1]
        scale = jnp.sqrt(jnp.asarray(C, dtype=q.dtype))
        energy = jnp.einsum('bcn,bcm->bnm', q, k) / scale
        attention = jax.nn.softmax(energy, axis=-1)
        x = jnp.einsum('bnm,bcm->bcn', attention, v)
        skip = jnp.einsum('oc,bcn->bon', Wskip, pcd_up)
        return skip + x

    def _L0_ffn_ref(x, qweight, scales, zeros, bias):
        import jax, jax.numpy as jnp
        import numpy as np
        B, S, IN, OUT = (4, 512, 1024, 1024)

        def _dequant_weight(qweight, scales, zeros):
            low = qweight & 15
            high = qweight >> 4 & 15
            w_int = jnp.stack([low, high], axis=1).reshape(-1, qweight.shape[1])
            zp = jnp.round(zeros / scales)
            return (w_int.astype(jnp.float32) - zp.T) * scales.T
        w = _dequant_weight(qweight, scales, zeros)
        y = jnp.einsum('bsi,io->bso', x.astype(jnp.float32), w) + bias
        return y.astype(x.dtype)
    x = x + _L0_xattn_ref(_layernorm(x, axis=-1), ctx_1024, L0_xattn_Wq, L0_xattn_Wk, L0_xattn_Wv, L0_xattn_Wskip)
    x = x + _L0_ffn_ref(_layernorm(x, axis=-1), L0_ffn_qweight, L0_ffn_scales, L0_ffn_zeros, L0_ffn_bias)
    return x

_drawn_inputs = setup_inputs


def setup_inputs(seed=0):
    import zlib

    import numpy as np

    out = dict(_drawn_inputs(seed))
    spreads = {}
    factors = {'L0_ffn_zeros': 8.0, 'L0_ffn_bias': 8.0}
    for name, (base, spread) in spreads.items():
        noise = np.random.default_rng([zlib.crc32(name.encode()), seed]).standard_normal(out[name].shape)
        drawn = base * np.exp(spread * noise) if base else spread * noise
        out[name] = jnp.asarray(drawn.astype(out[name].dtype))
    for name, factor in factors.items():
        out[name] = (out[name] * factor).astype(out[name].dtype)
    return out
```

```python
import numpy as np
import concourse.bass as bass
from concourse import mybir
from contextlib import ExitStack

F32 = mybir.dt.float32
F32R = mybir.dt.float32r
F16 = mybir.dt.float16
I32 = mybir.dt.int32
ALU = mybir.AluOpType
ACT = mybir.ActivationFunctionType
AX = mybir.AxisListType


def xattn_ffn_program(nc, x, ctx_in, wq, wk, wv, wskip, qweight, scales, zeros, bias, out):
    B, C, N = x.shape
    M = ctx_in.shape[2]
    OUT = qweight.shape[1]
    P = nc.NUM_PARTITIONS
    HALF = 512
    HALVES = N // HALF
    NT = N // P
    MT = M // P
    CHUNKS = 4
    TPC = NT // CHUNKS
    KT = N // P
    QT = qweight.shape[0] // P
    ZT = OUT // P
    EPS = 1e-5
    XN_SCALE = 1024.0
    SM_SCALE = 1.0 / float(np.sqrt(np.float32(C)))
    ROUND = float(2 ** 23)

    es = ExitStack()
    with es:
        def sb(name, shape, dt=F32):
            return es.enter_context(nc.sbuf_tensor("sb_" + name, shape, dt))

        def pb(name, shape, dt=F32):
            return es.enter_context(nc.psum_tensor("ps_" + name, shape, dt))

        def sem(name):
            return es.enter_context(nc.semaphore("s_" + name))

        def sems(name, n):
            return [sem(f"{name}{k}") for k in range(n)]

        wq_sb, wk_sb, wv_sb, wskip_sb = (sb(n, [C, C]) for n in ("wq", "wk", "wv", "wskip"))
        KEY, VAL, SKIP = range(3)
        proj_hi = sb("proj_hi", [C, 3, C], F32R)
        proj_lo = sb("proj_lo", [C, 3, C], F32R)
        ident = sb("ident", [P, P])
        neg_half = sb("neg_half", [P, 1])
        q_sb = sb("q", [P, QT, OUT], I32)
        nib_sb = sb("nib", [P, 2, OUT], I32)
        wf = sb("wf", [P, KT, OUT], F16)
        scale_row = sb("scale_row", [P, OUT])
        zps_row = sb("zps_row", [P, OUT])
        bias_row = sb("bias_row", [P, OUT])
        ones = sb("ones", [P, P])
        zp_sb = sb("zp", [P, 10, ZT])
        zp_small = sb("zp_small", [P, ZT], mybir.dt.uint32)
        zp_diag = sb("zp_diag", [P, ZT, P])

        x_sb = sb("x", [P, 2, N])
        ctx_sb = sb("ctx", [P, 2, M])
        ctx_hi, ctx_lo = (sb(n, [P, M], F32R) for n in ("ctx_hi", "ctx_lo"))
        xl = sb("xl", [P, N])
        xl_hi, xl_lo = (sb(n, [P, 2, N], F32R) for n in ("xl_hi", "xl_lo"))
        kv_hi, kv_lo = (sb(n, [P, 2, 2 * M], F32R) for n in ("kv_hi", "kv_lo"))
        prob = sb("prob", [P, CHUNKS, TPC, M])
        neg_max = sb("neg_max", [P, CHUNKS, TPC])
        esum = sb("esum", [P, CHUNKS, TPC])
        rsum = sb("rsum", [P, CHUNKS, TPC])
        pt_hi, pt_lo = (sb(n, [P, HALVES, MT, HALF], F32R) for n in ("pt_hi", "pt_lo"))
        x1 = sb("x1", [P, 2, N])
        xn = sb("xn", [P, N])
        xnt_hi, xnt_lo = (sb(n, [P, KT, P], F16) for n in ("xnt_hi", "xnt_lo"))
        rest = sb("rest", [P, 2, OUT])
        prod = sb("prod", [P, HALVES, HALF])
        o_sb = sb("o", [P, 2, OUT])
        st1, st2 = (sb(n, [P, HALVES, 6]) for n in ("st1", "st2"))
        mv1, mv2 = (sb(n, [P, 2]) for n in ("mv1", "mv2"))
        ve1, ve2, rstd1, rstd2 = (sb(n, [P, 1]) for n in ("ve1", "ve2", "rstd1", "rstd2"))
        nb1, nb2, rs2, spare = (sb(n, [P, 1]) for n in ("nb1", "nb2", "rs2", "spare"))

        ps_e = [pb(f"e{k}", [P, TPC, M]) for k in range(2)]
        ps_t = [pb(f"t{k}", [P, HALF]) for k in range(2)]
        ps_o = pb("o", [P, HALF])
        ps_kv = pb("kv", [P, 2 * M])
        ps_y = [pb(f"y{k}", [P, HALF]) for k in range(HALVES)]

        x_loaded, ctx_loaded, stored = sems("x_loaded", 2), sems("ctx_loaded", 2), sems("stored", 2)
        w_loaded, q_loaded, rows_loaded = sem("w_loaded"), sem("q_loaded"), sem("rows_loaded")
        ident_made, ident_zero = sem("ident_made"), sem("ident_zero")
        proj_done, proj_hi_done, proj_lo_done = sem("proj_done"), sem("proj_hi_done"), sem("proj_lo_done")
        nib_done, wf_done, zp_step, zs_loaded = sem("nib_done"), sem("wf_done"), sem("zp_step"), sem("zs_loaded")
        diag_done, zprow_done, rows_done = sem("diag_done"), sem("zprow_done"), sem("rows_done")
        mv1_done, st1_done, ve1_done, rstd1_done = (sem(n) for n in ("mv1", "st1", "ve1", "rstd1"))
        xl_done, xlhi_done, xllo_done = (sem(n) for n in ("xl", "xlhi", "xllo"))
        ctxhi_done, ctxlo_done, kv_done = sem("ctxhi"), sem("ctxlo"), sem("kv")
        kvhi_done, kvlo_done = sem("kvhi"), sem("kvlo")
        scores_done, max_done, exp_done = sems("scores", CHUNKS), sems("max", CHUNKS), sems("exp", CHUNKS)
        rsum_done, norm_done = sems("rsum", CHUNKS), sems("norm", CHUNKS)
        pt_done, pthi_done, ptlo_done = sems("pt", CHUNKS), sems("pthi", CHUNKS), sems("ptlo", CHUNKS)
        attn_done, x1_done = sems("attn", HALVES), sems("x1", HALVES)
        st2_done, mv2_done, ve2_done, rstd2_done = (sem(n) for n in ("st2", "mv2", "ve2", "rstd2"))
        nb1_done, nb2_done, xn_done = sem("nb1"), sem("nb2"), sem("xn")
        xnt_done, xnthi_done, xntlo_done = sems("xnt", HALVES), sems("xnthi", HALVES), sems("xntlo", HALVES)
        zpt_done, addx1_done, rest_done = sem("zpt"), sem("addx1"), sem("rest")
        y_done, prod_done, out_done = sems("y", HALVES), sems("prod", HALVES), sems("out", HALVES)

        def ran(b, back=0):
            return not isinstance(b, int) or 0 <= b - back < B

        def arrived(c, par, per=16):
            return (c - par) * (per // 2) + per

        def run_steps(eng, step):
            step(-1, 1)
            step(0, 0)
            step(1, 1)
            with eng.Fori(2, B - 3, 2) as b:
                step(b, 0)
                step(b + 1, 1)
            for b in range(B - 2, B + 2):
                step(b, b % 2)

        block = es.enter_context(nc.Block())

        @block.sync
        def _(sp):
            sp.dma_start(wk_sb[:, :], wk).then_inc(w_loaded, 16)
            sp.dma_start(wq_sb[:, :], wq).then_inc(w_loaded, 16)
            sp.dma_start(x_sb[:, 0, :], x[0, :, :]).then_inc(x_loaded[0], 16)
            sp.dma_start(ctx_sb[:, 0, :], ctx_in[0, :, :]).then_inc(ctx_loaded[0], 16)
            sp.dma_start(wv_sb[:, :], wv).then_inc(w_loaded, 16)
            sp.dma_start(wskip_sb[:, :], wskip).then_inc(w_loaded, 16)
            sp.dma_start(x_sb[:, 1, :], x[1, :, :]).then_inc(x_loaded[1], 16)
            sp.dma_start(ctx_sb[:, 1, :], ctx_in[1, :, :]).then_inc(ctx_loaded[1], 16)
            sp.dma_start(q_sb[:, :, :], qweight.rearrange("(t p) o -> p t o", p=P)).then_inc(q_loaded, 16)
            for k, src in enumerate((zeros, scales)):
                sp.dma_start(zp_sb[:, k, :], src.rearrange("a (p t) -> (a p) t", t=ZT)).then_inc(zs_loaded, 16)
            for row, src in ((scale_row, scales), (bias_row, bias)):
                sp.dma_start(row[:, :], src.broadcast_to((P, OUT))).then_inc(rows_loaded, 16)

            def step(b, par):
                q = b - 2
                if ran(q):
                    sp.wait_ge(out_done[0], q + 1)
                    sp.dma_start(out[q, :, 0:HALF], o_sb[:, par, 0:HALF]).then_inc(stored[par], 16)
                if ran(b) and ran(b + 2):
                    sp.wait_ge(ctxlo_done, b + 1)
                    sp.dma_start(ctx_sb[:, par, :], ctx_in[b + 2, :, :]).then_inc(ctx_loaded[par], 16)
                if ran(q):
                    sp.wait_ge(out_done[1], q + 1)
                    sp.dma_start(out[q, :, HALF:OUT], o_sb[:, par, HALF:OUT]).then_inc(stored[par], 16)
                if ran(b) and ran(b + 2):
                    sp.wait_ge(x1_done[1], b + 1)
                    sp.dma_start(x_sb[:, par, :], x[b + 2, :, :]).then_inc(x_loaded[par], 16)

            run_steps(sp, step)
            for par in range(2):
                sp.wait_ge(stored[par], 32 * (B // 2))

        @block.gpsimd
        def _(pool):
            pool.memset(ident[:, :], 0.0).then_inc(ident_zero, 1)
            pool.memset(ones[:, :], 1.0).then_inc(ident_made, 1)
            pool.memset(neg_half[:, :], -0.5).then_inc(ident_zero, 1)
            pool.wait_ge(ident_zero, 2)
            pool.affine_select(out=ident[:, :], in_=ident[:, :], compare_op=ALU.not_equal, fill=1.0,
                               base=0, pattern=[[-1, P]], channel_multiplier=1).then_inc(ident_made, 1)
            pool.wait_ge(ident_made, 2)

            def write_out(q, par, h):
                pool.wait_ge(prod_done[h], q + 1)
                if h == 0:
                    pool.wait_ge(rest_done, q + 1)
                    if ran(q, 2):
                        pool.wait_ge(stored[par], arrived(q - 2, par, 32))
                cols = slice(h * HALF, (h + 1) * HALF)
                pool.tensor_tensor(o_sb[:, par, cols], prod[:, h, :], rest[:, par, cols],
                                   ALU.add).then_inc(out_done[h], 1)

            def step(b, par):
                n, p, q = b + 1, b - 1, b - 2
                if ran(q):
                    write_out(q, par, 0)
                if ran(n):
                    pool.wait_ge(ctxhi_done, n + 1)
                    pool.tensor_tensor(ctx_lo[:, :], ctx_sb[:, 1 - par, :], ctx_hi[:, :].bitcast(F32),
                                       ALU.subtract).then_inc(ctxlo_done, 1)
                if ran(p):
                    r = rest[:, 1 - par, :]
                    pool.wait_ge(zpt_done, p + 1)
                    pool.tensor_tensor(r, r, x1[:, 1 - par, :], ALU.add).then_inc(addx1_done, 1)
                if ran(n):
                    pool.wait_ge(ve1_done, n + 1)
                    pool.tensor_tensor(rstd1[:, :], ve1[:, :], neg_half[:, :], ALU.pow).then_inc(rstd1_done, 1)
                if ran(p):
                    pool.wait_ge(addx1_done, p + 1)
                    if isinstance(p, int) and p == 0:
                        pool.wait_ge(rows_loaded, 32)
                    pool.tensor_tensor(r, r, bias_row[:, :], ALU.add).then_inc(rest_done, 1)
                if ran(n):
                    pool.wait_ge(xlhi_done, n + 1)
                    pool.tensor_tensor(xl_lo[:, 1 - par, :], xl[:, :], xl_hi[:, 1 - par, :].bitcast(F32),
                                       ALU.subtract).then_inc(xllo_done, 1)
                if ran(q):
                    write_out(q, par, 1)
                if ran(b):
                    pool.wait_ge(ve2_done, b + 1)
                    pool.tensor_tensor(rstd2[:, :], ve2[:, :], neg_half[:, :], ALU.pow).then_inc(rstd2_done, 1)

            run_steps(pool, step)

        @block.scalar
        def _(act):
            for k in (KEY, VAL, SKIP):
                act.wait_ge(proj_done, 3)
                act.activation(proj_hi[:, k, :], ps_t[0][:, k * C:(k + 1) * C], ACT.Copy,
                               scale=SM_SCALE if k == KEY else 1.0).then_inc(proj_hi_done, 1)

            def exps(b, j):
                act.wait_ge(max_done[j], b + 1)
                if ran(b, 1):
                    act.wait_ge(pt_done[j], b)
                for t in range(TPC):
                    done = act.activation(prob[:, j, t, :], ps_e[j % 2][:, t, :], ACT.Exp,
                                          bias=neg_max[:, j, t:t + 1], accum_out=esum[:, j, t:t + 1])
                done.then_inc(exp_done[j], 1)

            def probs_hi(b, j):
                h, cols = j // 2, slice((j % 2) * TPC * P, (j % 2 + 1) * TPC * P)
                act.wait_ge(pt_done[j], b + 1)
                if ran(b, 1):
                    act.wait_ge(attn_done[h], b)
                act.activation(pt_hi[:, h, :, cols], ps_t[j % 2][:, :].rearrange("p (m n) -> p m n", m=MT),
                               ACT.Copy).then_inc(pthi_done[j], 1)

            def unpack(t):
                act.wait_ge(nib_done, t + 1)
                act.activation(wf[:, 2 * t:2 * t + 2, :], nib_sb[:, :, :], ACT.Copy).then_inc(wf_done, 1)

            def step(b, par):
                n, p = b + 1, b - 1
                if ran(p):
                    act.wait_ge(nb2_done, p + 1)
                    if ran(p, 1):
                        act.wait_ge(xnt_done[1], p)
                    act.activation(xn[:, :], x1[:, 1 - par, :], ACT.Identity, bias=nb2[:, :],
                                   scale=rstd2[:, :], accum_out=rs2[:, :]).then_inc(xn_done, 1)
                if ran(b):
                    exps(b, 0)
                if ran(n):
                    act.wait_ge(ctx_loaded[1 - par], arrived(n, 1 - par))
                    if ran(n, 1):
                        act.wait_ge(kv_done, n)
                    act.activation(ctx_hi[:, :], ctx_sb[:, 1 - par, :], ACT.Copy).then_inc(ctxhi_done, 1)
                if ran(b):
                    exps(b, 1)
                if ran(p):
                    act.wait_ge(xn_done, p + 1)
                    if ran(p, 2):
                        act.wait_ge(out_done[1], p - 1)
                    if isinstance(p, int) and p == 0:
                        act.wait_ge(rows_done, 2)
                    act.activation(rest[:, 1 - par, :], zps_row[:, :], ACT.Copy,
                                   scale=rs2[:, :]).then_inc(zpt_done, 1)
                if ran(b):
                    exps(b, 2)
                    probs_hi(b, 0)
                    exps(b, 3)
                    probs_hi(b, 1)
                if isinstance(b, int) and b == 0:
                    unpack(0)
                if ran(b):
                    probs_hi(b, 2)
                if ran(n):
                    act.wait_ge(nb1_done, n + 1)
                    if ran(n, 1):
                        act.wait_ge(xllo_done, n)
                    act.activation(xl[:, :], x_sb[:, 1 - par, :], ACT.Identity, bias=nb1[:, :],
                                   scale=rstd1[:, :]).then_inc(xl_done, 1)
                    act.wait_ge(xl_done, n + 1)
                    act.activation(xl_hi[:, 1 - par, :], xl[:, :], ACT.Copy).then_inc(xlhi_done, 1)
                if isinstance(b, int) and b == 0:
                    unpack(1)
                if ran(b):
                    probs_hi(b, 3)
                if ran(p):
                    for h in range(HALVES):
                        act.wait_ge(xnt_done[h], p + 1)
                        if h == 0 and ran(p, 1):
                            act.wait_ge(y_done[1], p)
                        act.activation(xnt_hi[:, 4 * h:4 * h + 4, :],
                                       ps_t[h][:, :].rearrange("p (k r) -> p k r", r=P),
                                       ACT.Copy).then_inc(xnthi_done[h], 1)
                if ran(n):
                    act.wait_ge(kv_done, n + 1)
                    if ran(n, 2):
                        act.wait_ge(attn_done[1], n - 1)
                    act.activation(kv_hi[:, 1 - par, :], ps_kv[:, :], ACT.Copy).then_inc(kvhi_done, 1)
                if isinstance(b, int) and b == 0:
                    unpack(2)
                    unpack(3)

            run_steps(act, step)

        @block.vector
        def _(dve):
            def stats1(n, par, h):
                if h == 0:
                    dve.wait_ge(x_loaded[par], arrived(n, par))
                last = dve.bn_stats(st1[:, h, :], x_sb[:, par, h * HALF:(h + 1) * HALF])
                if h == HALVES - 1:
                    last.then_inc(st1_done, 1)

            def moments1(n):
                dve.wait_ge(st1_done, n + 1)
                dve.tensor_copy(spare[:, :], st1[:, 0, 0:1])
                dve.bn_aggr(mv1[:, :], st1[:, :, :]).then_inc(mv1_done, 1)
                dve.wait_ge(mv1_done, n + 1)
                dve.tensor_scalar(ve1[:, :], mv1[:, 1:2], EPS, 1.0, ALU.add, ALU.mult).then_inc(ve1_done, 1)

            def offset1(n):
                dve.wait_ge(rstd1_done, n + 1)
                if ran(n, 1):
                    dve.wait_ge(xl_done, n)
                dve.scalar_tensor_tensor(nb1[:, :], mv1[:, 0:1], -1.0, rstd1[:, :], ALU.mult,
                                         ALU.mult).then_inc(nb1_done, 1)

            def row_max(b, j):
                dve.wait_ge(scores_done[j], b + 1)
                dve.tensor_reduce(neg_max[:, j, :], ps_e[j % 2][:, :, :], AX.X, ALU.max,
                                  negate=True).then_inc(max_done[j], 1)

            def normalise(b, j):
                dve.wait_ge(exp_done[j], b + 1)
                dve.reciprocal(rsum[:, j, :], esum[:, j, :]).then_inc(rsum_done[j], 1)
                dve.wait_ge(rsum_done[j], b + 1)
                for t in range(TPC):
                    last = dve.tensor_scalar(prob[:, j, t, :], prob[:, j, t, :], rsum[:, j, t:t + 1], None,
                                             ALU.mult)
                last.then_inc(norm_done[j], 1)

            def probs_lo(b, j):
                h, cols = j // 2, slice((j % 2) * TPC * P, (j % 2 + 1) * TPC * P)
                dve.wait_ge(pthi_done[j], b + 1)
                dve.tensor_tensor(pt_lo[:, h, :, cols], ps_t[j % 2][:, :].rearrange("p (m n) -> p m n", m=MT),
                                  pt_hi[:, h, :, cols].bitcast(F32), ALU.subtract).then_inc(ptlo_done[j], 1)

            def scale_product(q, h):
                dve.wait_ge(y_done[h], q + 1)
                if ran(q, 1):
                    dve.wait_ge(out_done[h], q)
                dve.tensor_tensor(prod[:, h, :], ps_y[h][:, :], scale_row[:, h * HALF:(h + 1) * HALF],
                                  ALU.mult).then_inc(prod_done[h], 1)

            def residual(b, par, h):
                cols = slice(h * HALF, (h + 1) * HALF)
                dve.wait_ge(attn_done[h], b + 1)
                if h == 0 and ran(b, 2):
                    dve.wait_ge(addx1_done, b - 1)
                dve.tensor_tensor(x1[:, par, cols], ps_o[:, :], x_sb[:, par, cols],
                                  ALU.add).then_inc(x1_done[h], 1)

            def stats2(b, par, h):
                dve.wait_ge(x1_done[h], b + 1)
                last = dve.bn_stats(st2[:, h, :], x1[:, par, h * HALF:(h + 1) * HALF])
                if h == HALVES - 1:
                    last.then_inc(st2_done, 1)

            def moments2(b):
                dve.wait_ge(st2_done, b + 1)
                dve.tensor_copy(spare[:, :], st2[:, 0, 0:1])
                dve.bn_aggr(mv2[:, :], st2[:, :, :]).then_inc(mv2_done, 1)
                dve.wait_ge(mv2_done, b + 1)
                dve.tensor_scalar(ve2[:, :], mv2[:, 1:2], EPS, XN_SCALE ** -2, ALU.add,
                                  ALU.mult).then_inc(ve2_done, 1)

            def offset2(b):
                dve.wait_ge(rstd2_done, b + 1)
                if ran(b, 1):
                    dve.wait_ge(xn_done, b)
                dve.scalar_tensor_tensor(nb2[:, :], mv2[:, 0:1], -1.0, rstd2[:, :], ALU.mult,
                                         ALU.mult).then_inc(nb2_done, 1)

            def xn_lo(p, h):
                dve.wait_ge(xnthi_done[h], p + 1)
                dve.tensor_tensor(xnt_lo[:, 4 * h:4 * h + 4, :], ps_t[h][:, :].rearrange("p (k r) -> p k r", r=P),
                                  xnt_hi[:, 4 * h:4 * h + 4, :], ALU.subtract).then_inc(xntlo_done[h], 1)

            def nibbles(t):
                if t >= 1:
                    dve.wait_ge(wf_done, t)
                dve.wait_ge(q_loaded, 16)
                dve.tensor_scalar(nib_sb[:, 0, :], q_sb[:, t, :], 15, None, ALU.bitwise_and)
                dve.tensor_scalar(nib_sb[:, 1, :], q_sb[:, t, :], 4, 15, ALU.logical_shift_right,
                                  ALU.bitwise_and).then_inc(nib_done, 1)

            def zero_points():
                count = [0]

                def link(ins):
                    count[0] += 1
                    ins.then_inc(zp_step, 1)
                    dve.wait_ge(zp_step, count[0])

                def cut(hi, lo, v):
                    link(dve.tensor_scalar(hi.bitcast(I32), v.bitcast(I32), -4096, None, ALU.bitwise_and))
                    link(dve.tensor_tensor(lo, v, hi, ALU.subtract))

                z, s, recip, quot, qh, ql, sh, sl, rem, tmp = (zp_sb[:, k, :] for k in range(10))
                dve.wait_ge(zs_loaded, 32)
                link(dve.reciprocal(recip, s))
                link(dve.tensor_tensor(quot, z, recip, ALU.mult))
                cut(qh, ql, quot)
                cut(sh, sl, s)
                for n, (u, v) in enumerate(((qh, sh), (qh, sl), (ql, sh), (ql, sl))):
                    link(dve.tensor_tensor(tmp, u, v, ALU.mult))
                    link(dve.tensor_tensor(rem, z if n == 0 else rem, tmp, ALU.subtract))
                link(dve.tensor_tensor(tmp, rem, recip, ALU.mult))
                link(dve.tensor_tensor(quot, quot, tmp, ALU.add))
                link(dve.scalar_tensor_tensor(qh, quot, -1.0, quot, ALU.mult, ALU.max))
                link(dve.tensor_scalar(zp_small[:, :], qh, ROUND, None, ALU.is_lt))
                link(dve.tensor_scalar(qh, qh, ROUND, ROUND, ALU.add, ALU.subtract))
                link(dve.tensor_scalar(ql, quot, 0.0, 2.0, ALU.is_ge, ALU.mult))
                link(dve.tensor_scalar(ql, ql, 1.0, None, ALU.subtract))
                link(dve.tensor_tensor(qh, qh, ql, ALU.mult))
                link(dve.copy_predicated(quot, zp_small[:, :], qh))
                link(dve.scalar_tensor_tensor(rem, quot, -1.0 / XN_SCALE, s, ALU.mult, ALU.mult))
                dve.wait_ge(ident_made, 2)
                for t in range(ZT):
                    last = dve.tensor_scalar(zp_diag[:, t, :], ident[:, :], rem[:, t:t + 1], None, ALU.mult)
                last.then_inc(diag_done, 1)

            def zero_point_row():
                dve.wait_ge(zprow_done, 1)
                row = zps_row[:, :].rearrange("m (p t) -> m t p", t=ZT)
                for h in range(HALVES):
                    last = dve.tensor_copy(row[:, 4 * h:4 * h + 4, :],
                                           ps_y[h][:, :].rearrange("m (t p) -> m t p", p=P))
                last.then_inc(rows_done, 1)
                dve.wait_ge(rows_loaded, 32)
                dve.tensor_scalar(scale_row[:, :], scale_row[:, :], 1.0 / XN_SCALE, None,
                                  ALU.mult).then_inc(rows_done, 1)

            def step(b, par):
                n, p, q = b + 1, b - 1, b - 2
                first = isinstance(b, int) and b == 0
                if isinstance(b, int) and b == -1:
                    for k in (KEY, VAL, SKIP):
                        dve.wait_ge(proj_hi_done, 3)
                        dve.scalar_tensor_tensor(proj_lo[:, k, :], ps_t[0][:, k * C:(k + 1) * C],
                                                 SM_SCALE if k == KEY else 1.0,
                                                 proj_hi[:, k, :].bitcast(F32), ALU.mult,
                                                 ALU.subtract).then_inc(proj_lo_done, 1)
                if ran(q):
                    scale_product(q, 0)
                if ran(b):
                    row_max(b, 0)
                    row_max(b, 1)
                    normalise(b, 0)
                if ran(n):
                    stats1(n, 1 - par, 0)
                if ran(b):
                    row_max(b, 2)
                    normalise(b, 1)
                if ran(n):
                    stats1(n, 1 - par, 1)
                if ran(b):
                    row_max(b, 3)
                if ran(n):
                    moments1(n)
                if ran(b):
                    normalise(b, 2)
                    probs_lo(b, 0)
                if ran(n):
                    offset1(n)
                if ran(b):
                    normalise(b, 3)
                    probs_lo(b, 1)
                if first:
                    nibbles(0)
                if ran(q):
                    scale_product(q, 1)
                if ran(b):
                    probs_lo(b, 2)
                if first:
                    nibbles(1)
                    zero_points()
                if ran(b):
                    residual(b, par, 0)
                    probs_lo(b, 3)
                    stats2(b, par, 0)
                if ran(p):
                    xn_lo(p, 0)
                    xn_lo(p, 1)
                if ran(n):
                    dve.wait_ge(kvhi_done, n + 1)
                    dve.tensor_tensor(kv_lo[:, 1 - par, :], ps_kv[:, :], kv_hi[:, 1 - par, :].bitcast(F32),
                                      ALU.subtract).then_inc(kvlo_done, 1)
                if first:
                    nibbles(2)
                    nibbles(3)
                    zero_point_row()
                if ran(b):
                    residual(b, par, 1)
                    stats2(b, par, 1)
                    moments2(b)
                    offset2(b)

            run_steps(dve, step)

        @block.tensor
        def _(pe):
            HI_LO = ((0, 0), (0, 1), (1, 0))
            proj, ctx_p = (proj_hi, proj_lo), (ctx_hi, ctx_lo)
            xl_p, kv_p, pt_p, xnt_p = (xl_hi, xl_lo), (kv_hi, kv_lo), (pt_hi, pt_lo), (xnt_hi, xnt_lo)

            pe.wait_ge(w_loaded, 64)
            pe.wait_ge(ident_made, 2)
            pe.matmul(ps_t[0][:, 0:C], wk_sb[:, :], wq_sb[:, :], start=True, stop=True).then_inc(proj_done, 1)
            pe.transpose(ps_t[0][:, C:2 * C], wv_sb[:, :], ident[:, :]).then_inc(proj_done, 1)
            pe.transpose(ps_t[0][:, 2 * C:3 * C], wskip_sb[:, :], ident[:, :]).then_inc(proj_done, 1)

            def scores(b, par, j):
                if j >= 2:
                    pe.wait_ge(exp_done[j - 2], b + 1)
                elif ran(b, 1):
                    pe.wait_ge(exp_done[j + 2], b)
                for t in range(TPC):
                    cols = slice((j * TPC + t) * P, (j * TPC + t + 1) * P)
                    for n, (s, m) in enumerate(HI_LO):
                        last = pe.matmul(ps_e[j % 2][:, t, :], xl_p[s][:, par, cols], kv_p[m][:, par, 0:M],
                                         start=n == 0, stop=n == 2)
                last.then_inc(scores_done[j], 1)

            def transpose_probs(b, j):
                pe.wait_ge(norm_done[j], b + 1)
                if j >= 2:
                    pe.wait_ge(ptlo_done[j - 2], b + 1)
                elif ran(b, 1):
                    pe.wait_ge(ptlo_done[j + 2], b)
                if j < 2 and ran(b, 2):
                    pe.wait_ge(xntlo_done[j], b - 1)
                for m in range(MT):
                    for t in range(TPC):
                        last = pe.transpose(ps_t[j % 2][:, (m * TPC + t) * P:(m * TPC + t + 1) * P],
                                            prob[:, j, t, m * P:(m + 1) * P], ident[:, :])
                last.then_inc(pt_done[j], 1)

            def attend(b, par, h):
                cols = slice(h * HALF, (h + 1) * HALF)
                if h == 1:
                    pe.wait_ge(x1_done[0], b + 1)
                elif ran(b, 1):
                    pe.wait_ge(x1_done[1], b)
                for n, (s, m) in enumerate(HI_LO):
                    pe.matmul(ps_o[:, :], proj[s][:, SKIP, :], xl_p[m][:, par, cols], start=n == 0, stop=False)
                pe.wait_ge(ptlo_done[2 * h + 1], b + 1)
                for k in range(MT):
                    for n, (s, m) in enumerate(HI_LO):
                        last = pe.matmul(ps_o[:, :], kv_p[s][:, par, M + k * P:M + (k + 1) * P],
                                         pt_p[m][:, h, k, :], start=False, stop=k == MT - 1 and n == 2)
                last.then_inc(attn_done[h], 1)

            def transpose_xn(b, p):
                for h in range(HALVES):
                    if h == 0:
                        pe.wait_ge(xn_done, p + 1)
                    if ran(b):
                        pe.wait_ge(ptlo_done[2 + h], b + 1)
                    else:
                        pe.wait_ge(xntlo_done[h], p)
                    for k in range(4):
                        kt = 4 * h + k
                        t, e = kt // 2, kt % 2
                        last = pe.transpose(ps_t[h][:, k * P:(k + 1) * P],
                                            xn[:, 2 * P * t + e:2 * P * (t + 1):2], ident[:, :])
                    last.then_inc(xnt_done[h], 1)

            def ffn(c, h, g):
                if g == 0:
                    if h == 0:
                        pe.wait_ge(xntlo_done[0], c + 1)
                    if ran(c, 1):
                        pe.wait_ge(prod_done[h], c)
                if g == 2 and h == 0:
                    pe.wait_ge(xntlo_done[1], c + 1)
                if isinstance(c, int) and c == 0 and h == 0:
                    pe.wait_ge(wf_done, g + 1)
                    pe.wait_ge(rows_done, 2)
                for kt in (2 * g, 2 * g + 1):
                    for s in range(2):
                        last = pe.matmul(ps_y[h][:, :], xnt_p[s][:, kt, :], wf[:, kt, h * HALF:(h + 1) * HALF],
                                         start=kt == 0 and s == 0, stop=kt == KT - 1 and s == 1)
                if g == 3:
                    last.then_inc(y_done[h], 1)

            def keys_values(n, par):
                pe.wait_ge(ctxlo_done, n + 1)
                if ran(n, 1):
                    pe.wait_ge(kvlo_done, n)
                for k, (s, m) in enumerate(HI_LO):
                    pe.matmul(ps_kv[:, 0:M], proj[s][:, KEY, :], ctx_p[m][:, :], start=k == 0, stop=k == 2)
                for t in range(MT):
                    for k, (s, m) in enumerate(HI_LO):
                        last = pe.matmul(ps_kv[:, M + t * P:M + (t + 1) * P], ctx_p[s][:, t * P:(t + 1) * P],
                                         proj[m][:, VAL, :], start=k == 0, stop=k == 2)
                last.then_inc(kv_done, 1)

            def step(b, par):
                n, p, q = b + 1, b - 1, b - 2
                first = isinstance(b, int) and b == 0
                if isinstance(b, int) and b == -1:
                    pe.wait_ge(proj_lo_done, 3)
                if ran(b):
                    pe.wait_ge(kvlo_done, b + 1)
                    pe.wait_ge(xllo_done, b + 1)
                    scores(b, par, 0)
                if ran(q):
                    ffn(q, 1, 0)
                if ran(b):
                    scores(b, par, 1)
                if ran(q):
                    ffn(q, 1, 1)
                if ran(b):
                    scores(b, par, 2)
                if ran(q):
                    ffn(q, 1, 2)
                if ran(b):
                    transpose_probs(b, 0)
                    scores(b, par, 3)
                if ran(q):
                    ffn(q, 1, 3)
                if ran(b):
                    transpose_probs(b, 1)
                if ran(n):
                    keys_values(n, 1 - par)
                if ran(b):
                    transpose_probs(b, 2)
                    attend(b, par, 0)
                    transpose_probs(b, 3)
                if ran(p):
                    transpose_xn(b, p)
                if first:
                    pe.wait_ge(diag_done, 1)
                    for t in range(ZT):
                        last = pe.matmul(ps_y[t // 4][:, (t % 4) * P:(t % 4 + 1) * P], ones[:, :],
                                         zp_diag[:, t, :], start=True, stop=True)
                    last.then_inc(zprow_done, 1)
                if ran(b):
                    attend(b, par, 1)
                if ran(p):
                    for g in range(4):
                        ffn(p, 0, g)

            run_steps(pe, step)


_INS = ["x", "ctx_1024", "L0_xattn_Wq", "L0_xattn_Wk", "L0_xattn_Wv", "L0_xattn_Wskip",
        "L0_ffn_qweight", "L0_ffn_scales", "L0_ffn_zeros", "L0_ffn_bias"]


def kernel(**inputs):
    import concourse.bacc as bacc
    from concourse.bass_utils import run_bass_kernel_spmd

    nc = bacc.Bacc("TRN2", target_bir_lowering=False, num_devices=1)
    arrays, args = {}, []
    for name in _INS:
        a = np.ascontiguousarray(inputs[name])
        if name in ("L0_ffn_scales", "L0_ffn_zeros", "L0_ffn_bias"):
            a = a.reshape(1, -1)
        arrays[f"in_{name}_dram"] = a
        args.append(nc.dram_tensor(f"in_{name}_dram", a.shape, mybir.dt.from_np(a.dtype), kind="ExternalInput").ap())
    shape = inputs["x"].shape
    out = nc.dram_tensor("out_dram", shape, mybir.dt.float32, kind="ExternalOutput").ap()
    xattn_ffn_program(nc, *args, out)
    r = run_bass_kernel_spmd(nc, [arrays], core_ids=[0])
    return r.results[0]["out_dram"]
```

```python
import numpy as np
import concourse.bass as bass
from concourse import mybir
from contextlib import ExitStack

F32 = mybir.dt.float32
F32R = mybir.dt.float32r
F16 = mybir.dt.float16
I32 = mybir.dt.int32
ALU = mybir.AluOpType
ACT = mybir.ActivationFunctionType
AX = mybir.AxisListType


def xattn_ffn_program(nc, x, ctx_in, wq, wk, wv, wskip, qweight, scales, zeros, bias, out):
    B, C, N = x.shape
    M = ctx_in.shape[2]
    OUT = qweight.shape[1]
    P = nc.NUM_PARTITIONS
    HALF = 512
    HALVES = N // HALF
    NT = N // P
    MT = M // P
    CHUNKS = 4
    TPC = NT // CHUNKS
    KT = N // P
    QT = qweight.shape[0] // P
    ZT = OUT // P
    EPS = 1e-5
    XN_SCALE = 1024.0
    SM_SCALE = 1.0 / float(np.sqrt(np.float32(C)))
    ROUND = float(2 ** 23)

    es = ExitStack()
    with es:
        def sb(name, shape, dt=F32):
            return es.enter_context(nc.sbuf_tensor("sb_" + name, shape, dt))

        def pb(name, shape, dt=F32):
            return es.enter_context(nc.psum_tensor("ps_" + name, shape, dt))

        def sem(name):
            return es.enter_context(nc.semaphore("s_" + name))

        def sems(name, n):
            return [sem(f"{name}{k}") for k in range(n)]

        wq_sb, wk_sb, wv_sb, wskip_sb = (sb(n, [C, C]) for n in ("wq", "wk", "wv", "wskip"))
        KEY, VAL, SKIP = range(3)
        proj_hi = sb("proj_hi", [C, 3, C], F32R)
        proj_lo = sb("proj_lo", [C, 3, C], F32R)
        ident = sb("ident", [P, P])
        neg_half = sb("neg_half", [P, 1])
        q_sb = sb("q", [P, QT, OUT], I32)
        nib_sb = sb("nib", [P, 2, 2, OUT], I32)
        wf = sb("wf", [P, KT, OUT], F16)
        scale_row = sb("scale_row", [P, OUT])
        zps_row = sb("zps_row", [P, OUT])
        bias_row = sb("bias_row", [P, OUT])
        ones = sb("ones", [P, P])
        zp_sb = sb("zp", [P, 10, ZT])
        zp_small = sb("zp_small", [P, ZT], mybir.dt.uint32)
        zp_diag = sb("zp_diag", [P, ZT, P])

        x_sb = sb("x", [P, 2, N])
        ctx_sb = sb("ctx", [P, 2, M])
        ctx_hi, ctx_lo = (sb(n, [P, M], F32R) for n in ("ctx_hi", "ctx_lo"))
        xl = sb("xl", [P, N])
        xl_hi, xl_lo = (sb(n, [P, 2, N], F32R) for n in ("xl_hi", "xl_lo"))
        kv_hi, kv_lo = (sb(n, [P, 2, 2 * M], F32R) for n in ("kv_hi", "kv_lo"))
        prob = sb("prob", [P, CHUNKS, TPC, M])
        neg_max = sb("neg_max", [P, CHUNKS, TPC])
        esum = sb("esum", [P, CHUNKS, TPC])
        rsum = sb("rsum", [P, CHUNKS, TPC])
        pt_hi, pt_lo = (sb(n, [P, HALVES, MT, HALF], F32R) for n in ("pt_hi", "pt_lo"))
        x1 = sb("x1", [P, 2, N])
        xn = sb("xn", [P, N])
        xnt_hi, xnt_lo = (sb(n, [P, KT, P], F16) for n in ("xnt_hi", "xnt_lo"))
        rest = sb("rest", [P, 2, OUT])
        prod = sb("prod", [P, HALVES, HALF])
        o_sb = sb("o", [P, 2, OUT])
        st1, st2 = (sb(n, [P, HALVES, 6]) for n in ("st1", "st2"))
        mv1, mv2 = (sb(n, [P, 2]) for n in ("mv1", "mv2"))
        ve1, ve2, rstd1, rstd2 = (sb(n, [P, 1]) for n in ("ve1", "ve2", "rstd1", "rstd2"))
        nb1, nb2, rs2, spare = (sb(n, [P, 1]) for n in ("nb1", "nb2", "rs2", "spare"))

        ps_e = [pb(f"e{k}", [P, TPC, M]) for k in range(2)]
        ps_t = [pb(f"t{k}", [P, HALF]) for k in range(2)]
        ps_o = pb("o", [P, HALF])
        ps_kv = pb("kv", [P, 2 * M])
        ps_y = [pb(f"y{k}", [P, HALF]) for k in range(HALVES)]

        x_loaded, ctx_loaded, stored = sems("x_loaded", 2), sems("ctx_loaded", 2), sems("stored", 2)
        w_loaded, q_loaded, rows_loaded = sem("w_loaded"), sems("q_loaded", QT), sem("rows_loaded")
        ident_made, ident_zero = sem("ident_made"), sem("ident_zero")
        proj_done, proj_hi_done, proj_lo_done = sem("proj_done"), sem("proj_hi_done"), sem("proj_lo_done")
        nib_done, wf_done, zp_step, zs_loaded = sem("nib_done"), sem("wf_done"), sem("zp_step"), sem("zs_loaded")
        diag_done, zprow_done, rows_done = sem("diag_done"), sem("zprow_done"), sem("rows_done")
        mv1_done, st1_done, ve1_done, rstd1_done = (sem(n) for n in ("mv1", "st1", "ve1", "rstd1"))
        xl_done, xlhi_done, xllo_done = (sem(n) for n in ("xl", "xlhi", "xllo"))
        ctxhi_done, ctxlo_done, kv_done = sem("ctxhi"), sem("ctxlo"), sem("kv")
        kvhi_done, kvlo_done = sem("kvhi"), sem("kvlo")
        scores_done, max_done, exp_done = sems("scores", CHUNKS), sems("max", CHUNKS), sems("exp", CHUNKS)
        rsum_done, norm_done = sems("rsum", CHUNKS), sems("norm", CHUNKS)
        pt_done, pthi_done, ptlo_done = sems("pt", CHUNKS), sems("pthi", CHUNKS), sems("ptlo", CHUNKS)
        attn_done, x1_done = sems("attn", HALVES), sems("x1", HALVES)
        st2_done, mv2_done, ve2_done, rstd2_done = (sem(n) for n in ("st2", "mv2", "ve2", "rstd2"))
        nb1_done, nb2_done, xn_done = sem("nb1"), sem("nb2"), sem("xn")
        xnt_done, xnthi_done, xntlo_done = sems("xnt", HALVES), sems("xnthi", HALVES), sems("xntlo", HALVES)
        zpt_done, addx1_done, rest_done = sem("zpt"), sem("addx1"), sem("rest")
        y_done, prod_done, out_done = sems("y", HALVES), sems("prod", HALVES), sems("out", HALVES)

        def ran(b, back=0):
            return not isinstance(b, int) or 0 <= b - back < B

        def arrived(c, par, per=16):
            return (c - par) * (per // 2) + per

        def run_steps(eng, step, looped=4):
            for b in range(-1, looped):
                step(b, b % 2)
            with eng.Fori(looped, B - 3, 2) as b:
                step(b, 0)
                step(b + 1, 1)
            for b in range(B - 2, B + 3):
                step(b, b % 2)

        block = es.enter_context(nc.Block())

        @block.sync
        def _(sp):
            sp.dma_start(wk_sb[:, :], wk).then_inc(w_loaded, 16)
            sp.dma_start(wq_sb[:, :], wq).then_inc(w_loaded, 16)
            sp.dma_start(x_sb[:, 0, :], x[0, :, :]).then_inc(x_loaded[0], 16)
            sp.dma_start(ctx_sb[:, 0, :], ctx_in[0, :, :]).then_inc(ctx_loaded[0], 16)
            q_tiles = qweight.rearrange("(t p) o -> p t o", p=P)
            for t in range(QT):
                sp.dma_start(q_sb[:, t, :], q_tiles[:, t, :]).then_inc(q_loaded[t], 16)
                if t == 1:
                    sp.dma_start(x_sb[:, 1, :], x[1, :, :]).then_inc(x_loaded[1], 16)
                    sp.dma_start(ctx_sb[:, 1, :], ctx_in[1, :, :]).then_inc(ctx_loaded[1], 16)
            for row, src in ((scale_row, scales), (bias_row, bias)):
                sp.dma_start(row[:, :], src.broadcast_to((P, OUT))).then_inc(rows_loaded, 16)

            def step(b, par):
                c = b - 3
                if ran(c):
                    for h in range(HALVES):
                        sp.wait_ge(out_done[h], c + 1)
                        cols = slice(h * HALF, (h + 1) * HALF)
                        sp.dma_start(out[c, :, cols], o_sb[:, 1 - par, cols]).then_inc(stored[1 - par], 16)
                if ran(b) and ran(b + 2):
                    sp.wait_ge(ctxlo_done, b + 1)
                    sp.dma_start(ctx_sb[:, par, :], ctx_in[b + 2, :, :]).then_inc(ctx_loaded[par], 16)
                    sp.wait_ge(x1_done[1], b + 1)
                    sp.dma_start(x_sb[:, par, :], x[b + 2, :, :]).then_inc(x_loaded[par], 16)

            run_steps(sp, step)
            for par in range(2):
                sp.wait_ge(stored[par], 32 * (B // 2))

        @block.gpsimd
        def _(pool):
            pool.memset(ident[:, :], 0.0).then_inc(ident_zero, 1)
            pool.memset(ones[:, :], 1.0).then_inc(ident_made, 1)
            pool.memset(neg_half[:, :], -0.5).then_inc(ident_zero, 1)
            pool.wait_ge(ident_zero, 2)
            pool.affine_select(out=ident[:, :], in_=ident[:, :], compare_op=ALU.not_equal, fill=1.0,
                               base=0, pattern=[[-1, P]], channel_multiplier=1).then_inc(ident_made, 1)
            pool.wait_ge(ident_made, 2)

            def write_out(q, par, h):
                pool.wait_ge(prod_done[h], q + 1)
                if h == 0:
                    pool.wait_ge(rest_done, q + 1)
                    if ran(q, 2):
                        pool.wait_ge(stored[par], arrived(q - 2, par, 32))
                cols = slice(h * HALF, (h + 1) * HALF)
                pool.tensor_tensor(o_sb[:, par, cols], prod[:, h, :], rest[:, par, cols],
                                   ALU.add).then_inc(out_done[h], 1)

            def step(b, par):
                n, p, q, c = b + 1, b - 1, b - 2, b - 3
                if ran(c):
                    for h in range(HALVES):
                        write_out(c, 1 - par, h)
                if ran(q):
                    pool.wait_ge(addx1_done, q + 1)
                    if isinstance(q, int) and q == 0:
                        pool.wait_ge(rows_loaded, 32)
                    pool.tensor_tensor(rest[:, par, :], rest[:, par, :], bias_row[:, :],
                                       ALU.add).then_inc(rest_done, 1)
                if ran(n):
                    pool.wait_ge(ve1_done, n + 1)
                    pool.tensor_tensor(rstd1[:, :], ve1[:, :], neg_half[:, :], ALU.pow).then_inc(rstd1_done, 1)
                    pool.wait_ge(ctxhi_done, n + 1)
                    pool.tensor_tensor(ctx_lo[:, :], ctx_sb[:, 1 - par, :], ctx_hi[:, :].bitcast(F32),
                                       ALU.subtract).then_inc(ctxlo_done, 1)
                if ran(n):
                    pool.wait_ge(xlhi_done, n + 1)
                    pool.tensor_tensor(xl_lo[:, 1 - par, :], xl[:, :], xl_hi[:, 1 - par, :].bitcast(F32),
                                       ALU.subtract).then_inc(xllo_done, 1)
                if ran(p):
                    pool.wait_ge(zpt_done, p + 1)
                    pool.tensor_tensor(rest[:, 1 - par, :], rest[:, 1 - par, :], x1[:, 1 - par, :],
                                       ALU.add).then_inc(addx1_done, 1)
                if ran(b):
                    pool.wait_ge(ve2_done, b + 1)
                    pool.tensor_tensor(rstd2[:, :], ve2[:, :], neg_half[:, :], ALU.pow).then_inc(rstd2_done, 1)

            run_steps(pool, step, 6)

        @block.scalar
        def _(act):
            for k, src in enumerate((zeros, scales)):
                act.dma_start(zp_sb[:, k, :], src.rearrange("a (p t) -> (a p) t", t=ZT)).then_inc(zs_loaded, 16)
            for dst, src in ((wv_sb, wv), (wskip_sb, wskip)):
                act.dma_start(dst[:, :], src).then_inc(w_loaded, 16)
            for k in (KEY, VAL, SKIP):
                act.wait_ge(proj_done, 3)
                act.activation(proj_hi[:, k, :], ps_t[0][:, k * C:(k + 1) * C], ACT.Copy,
                               scale=SM_SCALE if k == KEY else 1.0).then_inc(proj_hi_done, 1)

            def exps(b, j):
                act.wait_ge(max_done[j], b + 1)
                if ran(b, 1):
                    act.wait_ge(pt_done[j], b)
                for t in range(TPC):
                    done = act.activation(prob[:, j, t, :], ps_e[j % 2][:, t, :], ACT.Exp,
                                          bias=neg_max[:, j, t:t + 1], accum_out=esum[:, j, t:t + 1])
                done.then_inc(exp_done[j], 1)

            def probs_hi(b, j):
                h, cols = j // 2, slice((j % 2) * TPC * P, (j % 2 + 1) * TPC * P)
                act.wait_ge(pt_done[j], b + 1)
                if ran(b, 1):
                    act.wait_ge(attn_done[h], b)
                act.activation(pt_hi[:, h, :, cols], ps_t[j % 2][:, :].rearrange("p (m n) -> p m n", m=MT),
                               ACT.Copy).then_inc(pthi_done[j], 1)

            def xn_hi(p, h):
                act.wait_ge(xnt_done[h], p + 1)
                if h == 0 and ran(p, 1):
                    act.wait_ge(y_done[1], p)
                act.activation(xnt_hi[:, 4 * h:4 * h + 4, :], ps_t[h][:, :].rearrange("p (k r) -> p k r", r=P),
                               ACT.Copy).then_inc(xnthi_done[h], 1)

            def unpack(t):
                act.wait_ge(nib_done, t + 1)
                act.activation(wf[:, 2 * t:2 * t + 2, :], nib_sb[:, t % 2, :, :], ACT.Copy).then_inc(wf_done, 1)

            def step(b, par):
                n, p = b + 1, b - 1
                if ran(b):
                    exps(b, 0)
                    exps(b, 1)
                if ran(p):
                    act.wait_ge(nb2_done, p + 1)
                    if ran(p, 1):
                        act.wait_ge(xnt_done[1], p)
                    act.activation(xn[:, :], x1[:, 1 - par, :], ACT.Identity, bias=nb2[:, :],
                                   scale=rstd2[:, :], accum_out=rs2[:, :]).then_inc(xn_done, 1)
                if ran(n):
                    act.wait_ge(ctx_loaded[1 - par], arrived(n, 1 - par))
                    if ran(n, 1):
                        act.wait_ge(kv_done, n)
                    act.activation(ctx_hi[:, :], ctx_sb[:, 1 - par, :], ACT.Copy).then_inc(ctxhi_done, 1)
                if ran(b):
                    exps(b, 2)
                    exps(b, 3)
                    probs_hi(b, 0)
                if ran(b):
                    probs_hi(b, 1)
                if ran(n):
                    act.wait_ge(nb1_done, n + 1)
                    if ran(n, 1):
                        act.wait_ge(xllo_done, n)
                    act.activation(xl[:, :], x_sb[:, 1 - par, :], ACT.Identity, bias=nb1[:, :],
                                   scale=rstd1[:, :]).then_inc(xl_done, 1)
                if ran(b):
                    probs_hi(b, 2)
                if ran(n):
                    act.wait_ge(xl_done, n + 1)
                    act.activation(xl_hi[:, 1 - par, :], xl[:, :], ACT.Copy).then_inc(xlhi_done, 1)
                if ran(b):
                    probs_hi(b, 3)
                if ran(p):
                    act.wait_ge(xn_done, p + 1)
                    if ran(p, 2):
                        act.wait_ge(out_done[1], p - 1)
                    if isinstance(p, int) and p == 0:
                        act.wait_ge(rows_done, 2)
                    act.activation(rest[:, 1 - par, :], zps_row[:, :], ACT.Copy,
                                   scale=rs2[:, :]).then_inc(zpt_done, 1)
                if ran(p):
                    xn_hi(p, 0)
                    xn_hi(p, 1)
                if ran(n):
                    act.wait_ge(kv_done, n + 1)
                    if ran(n, 2):
                        act.wait_ge(attn_done[1], n - 1)
                    act.activation(kv_hi[:, 1 - par, :], ps_kv[:, :], ACT.Copy).then_inc(kvhi_done, 1)
                if isinstance(b, int) and b == 0:
                    for t in range(QT):
                        unpack(t)

            run_steps(act, step)

        @block.vector
        def _(dve):
            def stats1(n, par, h):
                if h == 0:
                    dve.wait_ge(x_loaded[par], arrived(n, par))
                last = dve.bn_stats(st1[:, h, :], x_sb[:, par, h * HALF:(h + 1) * HALF])
                if h == HALVES - 1:
                    last.then_inc(st1_done, 1)

            def aggregate1(n):
                dve.wait_ge(st1_done, n + 1)
                dve.tensor_copy(spare[:, :], st1[:, 0, 0:1])
                dve.bn_aggr(mv1[:, :], st1[:, :, :]).then_inc(mv1_done, 1)

            def variance1(n):
                dve.wait_ge(mv1_done, n + 1)
                dve.tensor_scalar(ve1[:, :], mv1[:, 1:2], EPS, 1.0, ALU.add, ALU.mult).then_inc(ve1_done, 1)

            def offset1(n):
                dve.wait_ge(rstd1_done, n + 1)
                if ran(n, 1):
                    dve.wait_ge(xl_done, n)
                dve.scalar_tensor_tensor(nb1[:, :], mv1[:, 0:1], -1.0, rstd1[:, :], ALU.mult,
                                         ALU.mult).then_inc(nb1_done, 1)

            def row_max(b, j):
                dve.wait_ge(scores_done[j], b + 1)
                dve.tensor_reduce(neg_max[:, j, :], ps_e[j % 2][:, :, :], AX.X, ALU.max,
                                  negate=True).then_inc(max_done[j], 1)

            def invert(b, j):
                dve.wait_ge(exp_done[j], b + 1)
                dve.reciprocal(rsum[:, j, :], esum[:, j, :]).then_inc(rsum_done[j], 1)

            def normalise(b, j):
                dve.wait_ge(rsum_done[j], b + 1)
                for t in range(TPC):
                    last = dve.tensor_scalar(prob[:, j, t, :], prob[:, j, t, :], rsum[:, j, t:t + 1], None,
                                             ALU.mult)
                last.then_inc(norm_done[j], 1)

            def probs_lo(b, j):
                h, cols = j // 2, slice((j % 2) * TPC * P, (j % 2 + 1) * TPC * P)
                dve.wait_ge(pthi_done[j], b + 1)
                dve.tensor_tensor(pt_lo[:, h, :, cols], ps_t[j % 2][:, :].rearrange("p (m n) -> p m n", m=MT),
                                  pt_hi[:, h, :, cols].bitcast(F32), ALU.subtract).then_inc(ptlo_done[j], 1)

            def scale_product(q, h):
                dve.wait_ge(y_done[h], q + 1)
                if ran(q, 1):
                    dve.wait_ge(out_done[h], q)
                dve.tensor_tensor(prod[:, h, :], ps_y[h][:, :], scale_row[:, h * HALF:(h + 1) * HALF],
                                  ALU.mult).then_inc(prod_done[h], 1)

            def residual(b, par, h):
                cols = slice(h * HALF, (h + 1) * HALF)
                dve.wait_ge(attn_done[h], b + 1)
                if h == 0 and ran(b, 2):
                    dve.wait_ge(addx1_done, b - 1)
                dve.tensor_tensor(x1[:, par, cols], ps_o[:, :], x_sb[:, par, cols],
                                  ALU.add).then_inc(x1_done[h], 1)

            def stats2(b, par, h):
                dve.wait_ge(x1_done[h], b + 1)
                last = dve.bn_stats(st2[:, h, :], x1[:, par, h * HALF:(h + 1) * HALF])
                if h == HALVES - 1:
                    last.then_inc(st2_done, 1)

            def aggregate2(b):
                dve.wait_ge(st2_done, b + 1)
                dve.tensor_copy(spare[:, :], st2[:, 0, 0:1])
                dve.bn_aggr(mv2[:, :], st2[:, :, :]).then_inc(mv2_done, 1)

            def variance2(b):
                dve.wait_ge(mv2_done, b + 1)
                dve.tensor_scalar(ve2[:, :], mv2[:, 1:2], EPS, XN_SCALE ** -2, ALU.add,
                                  ALU.mult).then_inc(ve2_done, 1)

            def offset2(b):
                dve.wait_ge(rstd2_done, b + 1)
                if ran(b, 1):
                    dve.wait_ge(xn_done, b)
                dve.scalar_tensor_tensor(nb2[:, :], mv2[:, 0:1], -1.0, rstd2[:, :], ALU.mult,
                                         ALU.mult).then_inc(nb2_done, 1)

            def xn_lo(p, h):
                dve.wait_ge(xnthi_done[h], p + 1)
                dve.tensor_tensor(xnt_lo[:, 4 * h:4 * h + 4, :], ps_t[h][:, :].rearrange("p (k r) -> p k r", r=P),
                                  xnt_hi[:, 4 * h:4 * h + 4, :], ALU.subtract).then_inc(xntlo_done[h], 1)

            def nibbles(t):
                dve.wait_ge(q_loaded[t], 16)
                if t >= 2:
                    dve.wait_ge(wf_done, t - 1)
                dve.tensor_scalar(nib_sb[:, t % 2, 0, :], q_sb[:, t, :], 15, None, ALU.bitwise_and)
                dve.tensor_scalar(nib_sb[:, t % 2, 1, :], q_sb[:, t, :], 4, 15, ALU.logical_shift_right,
                                  ALU.bitwise_and).then_inc(nib_done, 1)

            def zero_points():
                count = [0]

                def link(ins):
                    count[0] += 1
                    ins.then_inc(zp_step, 1)
                    dve.wait_ge(zp_step, count[0])

                def cut(hi, lo, v):
                    link(dve.tensor_scalar(hi.bitcast(I32), v.bitcast(I32), -4096, None, ALU.bitwise_and))
                    link(dve.tensor_tensor(lo, v, hi, ALU.subtract))

                z, s, recip, quot, qh, ql, sh, sl, rem, tmp = (zp_sb[:, k, :] for k in range(10))
                dve.wait_ge(zs_loaded, 32)
                link(dve.reciprocal(recip, s))
                link(dve.tensor_tensor(quot, z, recip, ALU.mult))
                cut(qh, ql, quot)
                cut(sh, sl, s)
                for n, (u, v) in enumerate(((qh, sh), (qh, sl), (ql, sh), (ql, sl))):
                    link(dve.tensor_tensor(tmp, u, v, ALU.mult))
                    link(dve.tensor_tensor(rem, z if n == 0 else rem, tmp, ALU.subtract))
                link(dve.tensor_tensor(tmp, rem, recip, ALU.mult))
                link(dve.tensor_tensor(quot, quot, tmp, ALU.add))
                link(dve.scalar_tensor_tensor(qh, quot, -1.0, quot, ALU.mult, ALU.max))
                link(dve.tensor_scalar(zp_small[:, :], qh, ROUND, None, ALU.is_lt))
                link(dve.tensor_scalar(qh, qh, ROUND, ROUND, ALU.add, ALU.subtract))
                link(dve.tensor_scalar(ql, quot, 0.0, 2.0, ALU.is_ge, ALU.mult))
                link(dve.tensor_scalar(ql, ql, 1.0, None, ALU.subtract))
                link(dve.tensor_tensor(qh, qh, ql, ALU.mult))
                link(dve.copy_predicated(quot, zp_small[:, :], qh))
                link(dve.scalar_tensor_tensor(rem, quot, -1.0 / XN_SCALE, s, ALU.mult, ALU.mult))
                dve.wait_ge(ident_made, 2)
                for t in range(ZT):
                    last = dve.tensor_scalar(zp_diag[:, t, :], ident[:, :], rem[:, t:t + 1], None, ALU.mult)
                last.then_inc(diag_done, 1)

            def zero_point_row():
                dve.wait_ge(zprow_done, 1)
                row = zps_row[:, :].rearrange("m (p t) -> m t p", t=ZT)
                for h in range(HALVES):
                    last = dve.tensor_copy(row[:, 4 * h:4 * h + 4, :],
                                           ps_y[h][:, :].rearrange("m (t p) -> m t p", p=P))
                last.then_inc(rows_done, 1)
                dve.wait_ge(rows_loaded, 32)
                dve.tensor_scalar(scale_row[:, :], scale_row[:, :], 1.0 / XN_SCALE, None,
                                  ALU.mult).then_inc(rows_done, 1)

            def step(b, par):
                n, p, q = b + 1, b - 1, b - 2
                first = isinstance(b, int) and b == 0
                if isinstance(b, int) and b == -1:
                    zero_points()
                    for k in (KEY, VAL, SKIP):
                        dve.wait_ge(proj_hi_done, 3)
                        dve.scalar_tensor_tensor(proj_lo[:, k, :], ps_t[0][:, k * C:(k + 1) * C],
                                                 SM_SCALE if k == KEY else 1.0,
                                                 proj_hi[:, k, :].bitcast(F32), ALU.mult,
                                                 ALU.subtract).then_inc(proj_lo_done, 1)
                if ran(b):
                    row_max(b, 0)
                if ran(p):
                    offset2(p)
                if ran(b):
                    row_max(b, 1)
                    invert(b, 0)
                    normalise(b, 0)
                if ran(n):
                    stats1(n, 1 - par, 0)
                if ran(b):
                    row_max(b, 2)
                    invert(b, 1)
                    normalise(b, 1)
                    row_max(b, 3)
                if ran(n):
                    stats1(n, 1 - par, 1)
                if ran(b):
                    invert(b, 2)
                    normalise(b, 2)
                if ran(n):
                    aggregate1(n)
                    variance1(n)
                if ran(b):
                    invert(b, 3)
                    probs_lo(b, 0)
                    probs_lo(b, 1)
                    normalise(b, 3)
                if ran(n):
                    offset1(n)
                if ran(q):
                    scale_product(q, 0)
                    scale_product(q, 1)
                if ran(b):
                    probs_lo(b, 2)
                    residual(b, par, 0)
                    probs_lo(b, 3)
                    stats2(b, par, 0)
                if ran(p):
                    xn_lo(p, 0)
                    xn_lo(p, 1)
                if isinstance(b, int) and b == -1:
                    nibbles(0)
                    zero_point_row()
                if ran(n):
                    dve.wait_ge(kvhi_done, n + 1)
                    dve.tensor_tensor(kv_lo[:, 1 - par, :], ps_kv[:, :], kv_hi[:, 1 - par, :].bitcast(F32),
                                      ALU.subtract).then_inc(kvlo_done, 1)
                if isinstance(b, int) and b == -1:
                    nibbles(1)
                if ran(b):
                    residual(b, par, 1)
                    stats2(b, par, 1)
                    aggregate2(b)
                    variance2(b)
                if first:
                    nibbles(2)
                    nibbles(3)

            run_steps(dve, step)

        @block.tensor
        def _(pe):
            HI_LO = ((0, 0), (0, 1), (1, 0))
            proj, ctx_p = (proj_hi, proj_lo), (ctx_hi, ctx_lo)
            xl_p, kv_p, pt_p, xnt_p = (xl_hi, xl_lo), (kv_hi, kv_lo), (pt_hi, pt_lo), (xnt_hi, xnt_lo)

            pe.wait_ge(w_loaded, 64)
            pe.wait_ge(ident_made, 2)
            pe.matmul(ps_t[0][:, 0:C], wk_sb[:, :], wq_sb[:, :], start=True, stop=True).then_inc(proj_done, 1)
            pe.transpose(ps_t[0][:, C:2 * C], wv_sb[:, :], ident[:, :]).then_inc(proj_done, 1)
            pe.transpose(ps_t[0][:, 2 * C:3 * C], wskip_sb[:, :], ident[:, :]).then_inc(proj_done, 1)

            pe.wait_ge(diag_done, 1)
            for t in range(ZT):
                last = pe.matmul(ps_y[t // 4][:, (t % 4) * P:(t % 4 + 1) * P], ones[:, :], zp_diag[:, t, :],
                                 start=True, stop=True)
            last.then_inc(zprow_done, 1)

            def scores(b, par, j):
                if j >= 2:
                    pe.wait_ge(exp_done[j - 2], b + 1)
                elif ran(b, 1):
                    pe.wait_ge(exp_done[j + 2], b)
                for t in range(TPC):
                    cols = slice((j * TPC + t) * P, (j * TPC + t + 1) * P)
                    for n, (s, m) in enumerate(HI_LO):
                        last = pe.matmul(ps_e[j % 2][:, t, :], xl_p[s][:, par, cols], kv_p[m][:, par, 0:M],
                                         start=n == 0, stop=n == 2)
                last.then_inc(scores_done[j], 1)

            def transpose_probs(b, j):
                pe.wait_ge(norm_done[j], b + 1)
                if j >= 2:
                    pe.wait_ge(ptlo_done[j - 2], b + 1)
                elif ran(b, 1):
                    pe.wait_ge(ptlo_done[j + 2], b)
                if j < 2 and ran(b, 2):
                    pe.wait_ge(xntlo_done[j], b - 1)
                for m in range(MT):
                    for t in range(TPC):
                        last = pe.transpose(ps_t[j % 2][:, (m * TPC + t) * P:(m * TPC + t + 1) * P],
                                            prob[:, j, t, m * P:(m + 1) * P], ident[:, :])
                last.then_inc(pt_done[j], 1)

            def skip(b, par, h):
                cols = slice(h * HALF, (h + 1) * HALF)
                if h == 1:
                    pe.wait_ge(x1_done[0], b + 1)
                elif ran(b, 1):
                    pe.wait_ge(x1_done[1], b)
                for n, (s, m) in enumerate(HI_LO):
                    pe.matmul(ps_o[:, :], proj[s][:, SKIP, :], xl_p[m][:, par, cols], start=n == 0, stop=False)

            def attend(b, par, h):
                pe.wait_ge(ptlo_done[2 * h + 1], b + 1)
                for k in range(MT):
                    for n, (s, m) in enumerate(HI_LO):
                        last = pe.matmul(ps_o[:, :], kv_p[s][:, par, M + k * P:M + (k + 1) * P],
                                         pt_p[m][:, h, k, :], start=False, stop=k == MT - 1 and n == 2)
                last.then_inc(attn_done[h], 1)

            def transpose_xn(b, p, h):
                pe.wait_ge(xn_done, p + 1)
                if ran(b):
                    pe.wait_ge(ptlo_done[2 + h], b + 1)
                else:
                    pe.wait_ge(xntlo_done[h], p)
                for k in range(4):
                    t, e = (4 * h + k) // 2, k % 2
                    last = pe.transpose(ps_t[h][:, k * P:(k + 1) * P],
                                        xn[:, 2 * P * t + e:2 * P * (t + 1):2], ident[:, :])
                last.then_inc(xnt_done[h], 1)

            def ffn(c, h, g):
                if g == 0:
                    if h == 0:
                        pe.wait_ge(xntlo_done[0], c + 1)
                    if ran(c, 1):
                        pe.wait_ge(prod_done[h], c)
                if g == 2 and h == 0:
                    pe.wait_ge(xntlo_done[1], c + 1)
                if isinstance(c, int) and c == 0 and h == 0:
                    pe.wait_ge(wf_done, g + 1)
                    pe.wait_ge(rows_done, 2)
                for kt in (2 * g, 2 * g + 1):
                    for s in range(2):
                        last = pe.matmul(ps_y[h][:, :], xnt_p[s][:, kt, :], wf[:, kt, h * HALF:(h + 1) * HALF],
                                         start=kt == 0 and s == 0, stop=kt == KT - 1 and s == 1)
                if g == 3:
                    last.then_inc(y_done[h], 1)

            def keys_values(n, par):
                pe.wait_ge(ctxlo_done, n + 1)
                if ran(n, 1):
                    pe.wait_ge(kvlo_done, n)
                for k, (s, m) in enumerate(HI_LO):
                    pe.matmul(ps_kv[:, 0:M], proj[s][:, KEY, :], ctx_p[m][:, :], start=k == 0, stop=k == 2)
                for t in range(MT):
                    for k, (s, m) in enumerate(HI_LO):
                        last = pe.matmul(ps_kv[:, M + t * P:M + (t + 1) * P], ctx_p[s][:, t * P:(t + 1) * P],
                                         proj[m][:, VAL, :], start=k == 0, stop=k == 2)
                last.then_inc(kv_done, 1)

            def step(b, par):
                n, p, q = b + 1, b - 1, b - 2
                if isinstance(b, int) and b == -1:
                    pe.wait_ge(proj_lo_done, 3)
                if ran(b):
                    pe.wait_ge(kvlo_done, b + 1)
                    pe.wait_ge(xllo_done, b + 1)
                    scores(b, par, 0)
                if ran(q):
                    ffn(q, 0, 2)
                if ran(b):
                    scores(b, par, 1)
                if ran(q):
                    ffn(q, 0, 3)
                if ran(b):
                    scores(b, par, 2)
                if ran(q):
                    ffn(q, 1, 0)
                if ran(b):
                    scores(b, par, 3)
                if ran(q):
                    ffn(q, 1, 1)
                if ran(b):
                    transpose_probs(b, 0)
                if ran(q):
                    ffn(q, 1, 2)
                if ran(b):
                    transpose_probs(b, 1)
                    skip(b, par, 0)
                if ran(q):
                    ffn(q, 1, 3)
                if ran(b):
                    transpose_probs(b, 2)
                    attend(b, par, 0)
                    transpose_probs(b, 3)
                if ran(n):
                    keys_values(n, 1 - par)
                if ran(p):
                    transpose_xn(b, p, 0)
                if ran(b):
                    skip(b, par, 1)
                if ran(p):
                    transpose_xn(b, p, 1)
                if ran(b):
                    attend(b, par, 1)
                if ran(p):
                    ffn(p, 0, 0)
                    ffn(p, 0, 1)

            run_steps(pe, step)


_INS = ["x", "ctx_1024", "L0_xattn_Wq", "L0_xattn_Wk", "L0_xattn_Wv", "L0_xattn_Wskip",
        "L0_ffn_qweight", "L0_ffn_scales", "L0_ffn_zeros", "L0_ffn_bias"]


def kernel(**inputs):
    import concourse.bacc as bacc
    from concourse.bass_utils import run_bass_kernel_spmd

    nc = bacc.Bacc("TRN2", target_bir_lowering=False, num_devices=1)
    arrays, args = {}, []
    for name in _INS:
        a = np.ascontiguousarray(inputs[name])
        if name in ("L0_ffn_scales", "L0_ffn_zeros", "L0_ffn_bias"):
            a = a.reshape(1, -1)
        arrays[f"in_{name}_dram"] = a
        args.append(nc.dram_tensor(f"in_{name}_dram", a.shape, mybir.dt.from_np(a.dtype), kind="ExternalInput").ap())
    shape = inputs["x"].shape
    out = nc.dram_tensor("out_dram", shape, mybir.dt.float32, kind="ExternalOutput").ap()
    xattn_ffn_program(nc, *args, out)
    r = run_bass_kernel_spmd(nc, [arrays], core_ids=[0])
    return r.results[0]["out_dram"]
```
